# Optimizing a Trainium2 kernel written in Bass

```python
import numpy as np
import jax
import jax.numpy as jnp

def _softmax(x, axis=-1):
    return jax.nn.softmax(x, axis=axis)

def _gelu(x):
    return jax.nn.gelu(x, approximate=True)

def _silu(x):
    return jax.nn.silu(x)

def _sigmoid(x):
    return jax.nn.sigmoid(x)

def _layernorm(x, axis=-1, eps=1e-05):
    m = jnp.mean(x, axis=axis, keepdims=True)
    v = jnp.var(x, axis=axis, keepdims=True)
    return (x - m) / jnp.sqrt(v + eps)

def _scatter_add(tgt, idx, src, axis=0):
    return tgt.at[idx].add(src)

def _segment_sum(src, seg, n):
    return jax.ops.segment_sum(src, seg, n)
kernel_name = 'mk_prb_d1_jaxref_r4_1847a7'

def setup_inputs(seed: int=0):
    np.random.seed(seed)
    _w = jnp.asarray

    def _L0_attn_setup():
        import jax, jax.numpy as jnp
        import numpy as np
        EPS = 1e-05

        def _wkv_scan(k, v, w, u):
            eu = jnp.exp(u)

            def step(carry, kv):
                a, b = carry
                kt, vt = kv
                ek = jnp.exp(kt)
                euek = eu * ek
                out = (a + euek * vt) / (b + euek)
                return ((w * a + ek * vt, w * b + ek), out)
            B, T, C = k.shape
            init = (jnp.zeros((B, C), k.dtype), jnp.zeros((B, C), k.dtype))
            _, wkv = jax.lax.scan(step, init, (k.transpose(1, 0, 2), v.transpose(1, 0, 2)))
            return wkv.transpose(1, 0, 2)
        B, T, C = (4, 512, 512)
        key = jax.random.key(seed)
        ks = jax.random.split(key, 16)
        s = 1.0 / np.sqrt(C)
        inp = {'x': jax.random.normal(ks[0], (B, T, C), jnp.float32), 'time_decay': jax.random.uniform(ks[1], (C,), jnp.float32, -0.1, -0.01), 'time_first': jax.random.uniform(ks[2], (C,), jnp.float32, -0.1, 0.1), 'tm_k': jax.random.uniform(ks[3], (C,), jnp.float32), 'tm_v': jax.random.uniform(ks[4], (C,), jnp.float32), 'tm_r': jax.random.uniform(ks[5], (C,), jnp.float32), 'tm_g': jax.random.uniform(ks[6], (C,), jnp.float32), 'Wr': jax.random.normal(ks[7], (C, C), jnp.float32) * s, 'Wk': jax.random.normal(ks[8], (C, C), jnp.float32) * s, 'Wv': jax.random.normal(ks[9], (C, C), jnp.float32) * s, 'Wg': jax.random.normal(ks[10], (C, C), jnp.float32) * s, 'Wo': jax.random.normal(ks[11], (C, C), jnp.float32) * s, 'ln_g': jnp.ones((C,), jnp.float32), 'ln_b': jnp.zeros((C,), jnp.float32)}
        return inp
    _L0_attn_in = _L0_attn_setup()

    def _L0_ffn_setup():
        import jax, jax.numpy as jnp
        import numpy as np
        B, S, H = (2, 512, 512)
        E, K, F = (32, 4, 352)
        FS = 1408
        EPS = 1e-06
        CAP = 256
        key = jax.random.key(seed)
        ks = jax.random.split(key, 10)
        s = 0.02
        return {'hidden_states': jax.random.normal(ks[0], (B, S, H), jnp.float32), 'w_norm': 1.0 + 0.02 * jax.random.normal(ks[1], (H,), jnp.float32), 'w_router': s * jax.random.normal(ks[2], (H, E), jnp.float32), 'w_gate': s * jax.random.normal(ks[3], (E, H, F), jnp.float32), 'w_up': s * jax.random.normal(ks[4], (E, H, F), jnp.float32), 'w_down': s * jax.random.normal(ks[5], (E, F, H), jnp.float32), 'sw_gate': s * jax.random.normal(ks[6], (H, FS), jnp.float32), 'sw_up': s * jax.random.normal(ks[7], (H, FS), jnp.float32), 'sw_down': s * jax.random.normal(ks[8], (FS, H), jnp.float32), 'w_shared_gate': s * jax.random.normal(ks[9], (H, 1), jnp.float32)}
    _L0_ffn_in = _L0_ffn_setup()
    _d = {'L0_attn_x': _L0_attn_in['x'], 'L0_attn_time_decay': _L0_attn_in['time_decay'], 'L0_attn_time_first': _L0_attn_in['time_first'], 'L0_attn_tm_k': _L0_attn_in['tm_k'], 'L0_attn_tm_v': _L0_attn_in['tm_v'], 'L0_attn_tm_r': _L0_attn_in['tm_r'], 'L0_attn_tm_g': _L0_attn_in['tm_g'], 'L0_attn_Wr': _L0_attn_in['Wr'], 'L0_attn_Wk': _L0_attn_in['Wk'], 'L0_attn_Wv': _L0_attn_in['Wv'], 'L0_attn_Wg': _L0_attn_in['Wg'], 'L0_attn_Wo': _L0_attn_in['Wo'], 'L0_attn_ln_g': _L0_attn_in['ln_g'], 'L0_attn_ln_b': _L0_attn_in['ln_b'], 'L0_ffn_w_norm': _L0_ffn_in['w_norm'], 'L0_ffn_w_router': _L0_ffn_in['w_router'], 'L0_ffn_w_gate': _L0_ffn_in['w_gate'], 'L0_ffn_w_up': _L0_ffn_in['w_up'], 'L0_ffn_w_down': _L0_ffn_in['w_down'], 'L0_ffn_sw_gate': _L0_ffn_in['sw_gate'], 'L0_ffn_sw_up': _L0_ffn_in['sw_up'], 'L0_ffn_sw_down': _L0_ffn_in['sw_down'], 'L0_ffn_w_shared_gate': _L0_ffn_in['w_shared_gate']}
    _x0 = _d['L0_attn_x']
    _d['L0_attn_x'] = jax.random.normal(jax.random.fold_in(jax.random.key(seed), 1), (8, 512, 512), dtype=_x0.dtype)
    del _x0
    return _d

def reference(L0_attn_x, L0_attn_time_decay, L0_attn_time_first, L0_attn_tm_k, L0_attn_tm_v, L0_attn_tm_r, L0_attn_tm_g, L0_attn_Wr, L0_attn_Wk, L0_attn_Wv, L0_attn_Wg, L0_attn_Wo, L0_attn_ln_g, L0_attn_ln_b, L0_ffn_w_norm, L0_ffn_w_router, L0_ffn_w_gate, L0_ffn_w_up, L0_ffn_w_down, L0_ffn_sw_gate, L0_ffn_sw_up, L0_ffn_sw_down, L0_ffn_w_shared_gate):

    def _L0_attn_ref(x, time_decay, time_first, tm_k, tm_v, tm_r, tm_g, Wr, Wk, Wv, Wg, Wo, ln_g, ln_b):
        import jax, jax.numpy as jnp
        import numpy as np
        EPS = 1e-05

        def _wkv_scan(k, v, w, u):
            eu = jnp.exp(u)

            def step(carry, kv):
                a, b = carry
                kt, vt = kv
                ek = jnp.exp(kt)
                euek = eu * ek
                out = (a + euek * vt) / (b + euek)
                return ((w * a + ek * vt, w * b + ek), out)
            B, T, C = k.shape
            init = (jnp.zeros((B, C), k.dtype), jnp.zeros((B, C), k.dtype))
            _, wkv = jax.lax.scan(step, init, (k.transpose(1, 0, 2), v.transpose(1, 0, 2)))
            return wkv.transpose(1, 0, 2)
        prev = jnp.concatenate([x[:, 1:2, :], x[:, :-1, :]], axis=1)
        xx = prev - x
        xk = x + xx * tm_k
        xv = x + xx * tm_v
        xr = x + xx * tm_r
        xg = x + xx * tm_g
        r = xr @ Wr.T
        k = xk @ Wk.T
        v = xv @ Wv.T
        g = jax.nn.sigmoid(xg @ Wg.T)
        w = jnp.exp(-jnp.exp(time_decay))
        wkv = _wkv_scan(k, v, w, time_first)
        attn = jax.nn.sigmoid(r) * wkv
        o = attn * g @ Wo.T
        mu = o.mean(-1, keepdims=True)
        var = ((o - mu) ** 2).mean(-1, keepdims=True)
        return (o - mu) * jax.lax.rsqrt(var + EPS) * ln_g + ln_b

    def _L0_ffn_ref(hidden_states, w_norm, w_router, w_gate, w_up, w_down, sw_gate, sw_up, sw_down, w_shared_gate):
        import jax, jax.numpy as jnp
        import numpy as np
        B, S, H = (2, 512, 512)
        E, K, F = (32, 4, 352)
        FS = 1408
        EPS = 1e-06
        CAP = 256
        inp = hidden_states
        xf = inp.astype(jnp.float32)
        var = jnp.mean(xf * xf, axis=-1, keepdims=True)
        x = (w_norm * (xf * jax.lax.rsqrt(var + EPS))).astype(inp.dtype)
        Bq, Sq, Hq = x.shape
        x = x.reshape(-1, Hq)
        T = Bq * Sq
        logits = x @ w_router
        probs = jax.nn.softmax(logits.astype(jnp.float32), axis=-1)
        w_topk, sel = jax.lax.top_k(probs, K)
        w_topk = w_topk.astype(x.dtype)
        flat_e = sel.reshape(-1)
        order = jnp.argsort(flat_e)
        sorted_e = flat_e[order]
        counts = jnp.zeros((E,), jnp.int32).at[flat_e].add(1)
        starts = jnp.cumsum(counts) - counts
        pos = jnp.arange(T * K) - starts[sorted_e]
        tok = order // K
        valid = pos < CAP
        dest = jnp.where(valid, pos, CAP)
        buf = jnp.zeros((E, CAP + 1, Hq), x.dtype).at[sorted_e, dest].set(x[tok])
        buf = buf[:, :CAP]
        g = jnp.einsum('ech,ehf->ecf', buf, w_gate)
        u = jnp.einsum('ech,ehf->ecf', buf, w_up)
        y = jnp.einsum('ecf,efh->ech', jax.nn.silu(g) * u, w_down)
        wv = w_topk.reshape(-1)[order] * valid.astype(x.dtype)
        gath = y[sorted_e, jnp.minimum(pos, CAP - 1)]
        out = jnp.zeros((T, Hq), x.dtype).at[tok].add(gath * wv[:, None])
        sh = jax.nn.silu(x @ sw_gate) * (x @ sw_up) @ sw_down
        sh = jax.nn.sigmoid(x @ w_shared_gate) * sh
        out = out + sh
        return inp + out.reshape(Bq, Sq, Hq)
    x = L0_attn_x
    xn = _layernorm(x, axis=-1)
    x = x + _L0_attn_ref(xn, L0_attn_time_decay, L0_attn_time_first, L0_attn_tm_k, L0_attn_tm_v, L0_attn_tm_r, L0_attn_tm_g, L0_attn_Wr, L0_attn_Wk, L0_attn_Wv, L0_attn_Wg, L0_attn_Wo, L0_attn_ln_g, L0_attn_ln_b) + _L0_ffn_ref(xn, L0_ffn_w_norm, L0_ffn_w_router, L0_ffn_w_gate, L0_ffn_w_up, L0_ffn_w_down, L0_ffn_sw_gate, L0_ffn_sw_up, L0_ffn_sw_down, L0_ffn_w_shared_gate)
    return x

_drawn_inputs = setup_inputs


def setup_inputs(seed=0):
    import zlib

    import numpy as np

    out = dict(_drawn_inputs(seed))
    spreads = {'L0_attn_ln_g': (1.0, 0.2), 'L0_attn_ln_b': (0.0, 0.1)}
    factors = {}
    for name, (base, spread) in spreads.items():
        noise = np.random.default_rng([zlib.crc32(name.encode()), seed]).standard_normal(out[name].shape)
        drawn = base * np.exp(spread * noise) if base else spread * noise
        out[name] = jnp.asarray(drawn.astype(out[name].dtype))
    for name, factor in factors.items():
        out[name] = (out[name] * factor).astype(out[name].dtype)
    return out
```

```python
from contextlib import ExitStack

import concourse.bass as bass
import numpy as np
from concourse import mybir

F32 = mybir.dt.float32
F32R = mybir.dt.float32r
BF16 = mybir.dt.bfloat16
U32 = mybir.dt.uint32
ALU = mybir.AluOpType
ACT = mybir.ActivationFunctionType
AX = mybir.AxisListType

P = 128
B, T, C = 8, 512, 512
KC = C // P
NT = T // P
E, TOPK, CAP = 32, 4, 256
F, FS = 352, 1408
NCT = CAP // P
SLOTS = E * CAP
ROW = SLOTS // P
RW = E + 2
FT = [(f, min(P, F - f)) for f in range(0, F, P)]
NFS = FS // P
EPS, EPS_RMS = 1e-5, 1e-6
DROPPED = 1 << 20
REC = 2 * NT + NT * TOPK + NT
K_, V_, R_, G_, O_ = range(5)
PRODUCTS = ((1, 0), (0, 1), (0, 0))


def wait(eng, sem, value):
    if not (isinstance(value, int) and value <= 0):
        eng.wait_ge(sem, value)


def wait_apart(eng, met, sem, value):
    if not isinstance(value, int):
        value = eng.to_reg(value)
    eng.wait_ge(*met)
    wait(eng, sem, value)


class Steps:

    def __init__(self, eng, sem, per):
        self.eng, self.sem, self.per = eng, sem, per

    def round(self, r, taken=0):
        self.base, self.n = r * self.per, taken

    def step(self, ins):
        ins.then_inc(self.sem, 1)
        self.n += 1
        assert self.n <= self.per, (self.n, self.per)

    def join(self):
        self.eng.wait_ge(self.sem, self.base + self.n)

    def join_apart(self, met):
        wait_apart(self.eng, met, self.sem, self.base + self.n)

    def link(self, ins):
        self.step(ins)
        self.join()

    def end(self):
        assert self.n == self.per, (self.n, self.per)


def attention_stage(nc, keep, d):
    with ExitStack() as ctx:
        def sb(name, shape, dt=F32):
            return ctx.enter_context(nc.sbuf_tensor(name, shape, dt))

        def psum(name):
            return ctx.enter_context(nc.psum_tensor(name, [P, 512], F32))

        def sem(name):
            return ctx.enter_context(nc.semaphore(name))

        w = [sb(f"w{i}", [P, 2, KC, C], F32R) for i in range(5)]
        wr = sb("wr", [P, KC, 2, RW], F32R)
        wr_in = sb("wr_in", [P, KC, RW])
        tm = sb("tm", [P, 4, KC])
        u_in = sb("u_in", [P, 2, KC])
        u_mid = sb("u_mid", [P, KC])
        decay = sb("decay", [P, KC])
        first = sb("first", [P, KC])
        norm_w = sb("norm_w", [P, C])
        const = sb("const", [P, 2 * P + E + NT])
        ident = const[:, 0:P]
        before_in = const[:, P:2 * P]
        expert_id = const[:, 2 * P:2 * P + E]
        token_id = const[:, 2 * P + E:2 * P + E + NT]
        before = sb("before", [P, P], BF16)
        ones = sb("ones", [P, P], BF16)
        mhalf = sb("mhalf", [P, NT])
        x_in = sb("x_in", [P, NT, C])
        xn = sb("xn", [P, 2, C])
        z = sb("z", [P, 2, C])
        xnT = sb("xnT", [P, 2, KC, T + 1])
        xx = sb("xx", [P, KC, T])
        zT = sb("zT", [P, 2, 2, KC, P], F32R)
        mixf = sb("mixf", [P, 2, T])
        mix = sb("mix", [P, KC, 2, T], F32R)
        ek = sb("ek", [P, KC, T])
        ekv = sb("ekv", [P, KC, T])
        sr = sb("sr", [P, KC, T])
        a_sum = sb("a_sum", [P, T + 1])
        b_sum = sb("b_sum", [P, T + 1])
        den = sb("den", [P, T])
        evac = sb("evac", [P, 4, T])
        att = sb("att", [P, 2, 2, T], F32R)
        st = sb("st", [P, NT, 6])
        mv = sb("mv", [P, NT, 2])
        var_eps = sb("var_eps", [P, NT])
        r2 = sb("r2", [P, NT])
        scales = sb("scales", [P, 2 * NT])
        rec = sb("rec", [P, REC - 2 * NT])
        lg = sb("lg", [P, NT, RW])
        v8 = sb("v8", [P, NT, 8])
        i8 = sb("i8", [P, NT, 8], U32)
        sh = sb("sh", [P, NT, E + TOPK + 1])
        ex = sb("ex", [P, NT, E + TOPK + 1])
        idxf = sb("idxf", [P, NT * TOPK])
        oh = sb("oh", [P, NT * TOPK, E])
        chosen = sb("chosen", [P, NT, E], BF16)
        seen = sb("seen", [P, NT + 1, E], BF16)
        pos = sb("pos", [P, NT * TOPK])
        valid = sb("valid", [P, NT * TOPK])
        bad = sb("bad", [P, NT * TOPK])
        second = sb("second", [P, NT * TOPK])
        s1 = sb("s1", [P, NT * TOPK])
        s2 = sb("s2", [P, NT * TOPK])
        slot = sb("slot", [P, NT * TOPK], U32)
        token = sb("token", [P, NT], U32)
        tot = sb("tot", [P, NT, 2])
        rtot = sb("rtot", [P, NT, 2])
        zero_tab = sb("zero_tab", [P, ROW], U32)

        pj = [psum(f"pj{m}") for m in range(4)]
        ta = psum("ta")
        tz = [psum(f"tz{i}") for i in range(2)]
        rp = psum("rp")
        rp_lg = rp[:, 0:NT * 2 * RW]
        rp_pos = rp[:, 512 - NT * E:512]

        c_loaded = sem("c_loaded")
        w_loaded = [sem(f"w_loaded{i}") for i in range(5)]
        w_hi, w_lo = sem("w_hi"), sem("w_lo")
        setup_dve, setup_act, setup_pool = sem("setup_dve"), sem("setup_act"), sem("setup_pool")
        table_zeroed = sem("table_zeroed")
        x_loaded = [sem(f"x_loaded{j}") for j in range(NT)]
        stats_step, pow_step = sem("stats_step"), sem("pow_step")
        xn_made, z_made = sem("xn_made"), sem("z_made")
        xn_turned, z_turned = sem("xn_turned"), sem("z_turned")
        xnT_made, zh_made, zl_made = sem("xnT_made"), sem("zh_made"), sem("zl_made")
        z_stored = [sem(f"z_stored{i}") for i in range(2)]
        zT_stored = [sem(f"zT_stored{i}") for i in range(2)]
        o_stored = [sem(f"o_stored{i}") for i in range(2)]
        scores_made, sh_made, rexp_made = sem("scores_made"), sem("sh_made"), sem("rexp_made")
        route_step, slot_made, rec_made = sem("route_step"), sem("slot_made"), sem("rec_made")
        lg_low = sem("lg_low")
        lg_made, chosen_made, pos_made, pos_read = sem("lg_made"), sem("chosen_made"), sem("pos_made"), sem("pos_read")
        scattered = sem("scattered")
        xx_made, mix_made, hi_made, lo_made, mix_used = (sem("xx_made"), sem("mix_made"), sem("hi_made"),
                                                         sem("lo_made"), sem("mix_used"))
        k_done, v_done, r_done, g_done, o_done = (sem(f"{n}_done") for n in "kvrgo")
        proj_done = [k_done, v_done, r_done, g_done, o_done]
        scales_kept = sem("scales_kept")
        ek_made, ekv_made, sr_made, sg_made = sem("ek_made"), sem("ekv_made"), sem("sr_made"), sem("sg_made")
        wkv_step, gate_made, att_made = sem("wkv_step"), sem("gate_made"), sem("att_made")
        ah_made, al_made, att_used, o_made = sem("ah_made"), sem("al_made"), sem("att_used"), sem("o_made")

        stage = [ek[:], ekv[:], sr[:], evac[:], evac[:]]
        STATS, POWS, ROUTES, CHOOSE, WKV = 8, 8, 22, 15, 24

        block = ctx.enter_context(nc.Block())

        def rounds(eng, one_round):
            one_round(0, 0, True, False)
            with eng.Fori(0, B // 2 - 1) as h:
                one_round(h * 2 + 1, 1, True, True)
                one_round(h * 2 + 2, 0, True, True)
            one_round(B - 1, 1, False, True)

        @block.sync
        def _(sp):
            def load_x(b, j):
                wait(sp, xn_made, b * NT + j + 1 - NT)
                sp.dma_start(x_in[:, j, :], d["x_tile"](b, j)).then_inc(x_loaded[j], 16)

            def store_z(b, j):
                sp.wait_ge(z_made, b * NT + j + 1)
                sp.dma_start(d["z_tile"](b, j), z[:, j % 2, :]).then_inc(z_stored[j % 2], 16)

            def store_zT(b, j):
                sp.wait_ge(zl_made, b * NT + j + 1)
                sp.dma_start(d["zT_tile"](b, j), zT[:, j % 2].bitcast(F32)).then_inc(zT_stored[j % 2], 16)

            def store_o(b, j):
                sp.wait_ge(o_made, b * NT + j + 1)
                sp.dma_start(d["o_tile"](b, j), evac[:, j, :]).then_inc(o_stored[j % 2], 16)

            for j in range(NT):
                load_x(0, j)
            sp.dma_start(const[:], d["const"]).then_inc(c_loaded, 16)
            for i, name in enumerate(("tm_k", "tm_v", "tm_r", "tm_g")):
                sp.dma_start(tm[:, i, :], d[name].rearrange("(p k) -> p k", k=KC)).then_inc(c_loaded, 16)
            with nc.allow_non_contiguous_dma(reason="512 values once"):
                for i, name in enumerate(("time_decay", "time_first")):
                    sp.dma_start(u_in[:, i, :], d[name].rearrange("(m p) -> p m", p=P)).then_inc(c_loaded, 16)
                sp.dma_start(wr_in[:, :, E:E + 1],
                             d["w_shared_gate"].rearrange("(p k) n -> p k n", k=KC)).then_inc(c_loaded, 16)
            sp.dma_start(wr_in[:, :, 0:E], d["w_router"].rearrange("(p k) n -> p k n", k=KC)).then_inc(c_loaded, 16)
            sp.dma_start(norm_w[:], d["w_norm"].rearrange("(o c) -> o c", o=1).to_broadcast([P, C])).then_inc(c_loaded, 16)
            names = ("Wk", "Wv", "Wr", "Wg", "Wo")
            for i in (K_, V_, R_, G_):
                sp.dma_start(stage[i], d[names[i]].rearrange("(p k) n -> p k n", k=KC)).then_inc(w_loaded[i], 16)
            sp.wait_ge(setup_pool, 1)
            sp.dma_start(d["table"], zero_tab[:]).then_inc(table_zeroed, 16)
            for pair in ((0, 1), (2, 3)):
                for j in pair:
                    store_z(0, j)
                for j in pair:
                    store_zT(0, j)

            def one_round(b, half, more, before):
                if more:
                    for j in range(NT):
                        load_x(b + 1, j)
                    for j in (0, 1):
                        store_z(b + 1, j)
                    for j in (0, 1):
                        store_zT(b + 1, j)
                    for j in (2, 3):
                        store_z(b + 1, j)
                if before:
                    for j in range(NT):
                        store_o(b - 1, j)
                else:
                    sp.wait_ge(w_lo, 4)
                    sp.dma_start(stage[O_], d["Wo"].rearrange("(m p) n -> p m n", p=P)).then_inc(w_loaded[O_], 16)
                if more:
                    for j in (2, 3):
                        store_zT(b + 1, j)

            rounds(sp, one_round)
            for j in range(NT):
                store_o(B - 1, j)
            for i in range(2):
                sp.wait_ge(z_stored[i], 16 * B * NT // 2)
                sp.wait_ge(zT_stored[i], 16 * B * NT // 2)
                sp.wait_ge(o_stored[i], 16 * B * NT // 2)

        @block.gpsimd
        def _(pool):
            pows = Steps(pool, pow_step, POWS)

            def norm_scales(b):
                wait(pool, scales_kept, b)
                wait(pool, z_made, b * NT)
                wait_apart(pool, (setup_pool, 6), stats_step, (b + 1) * STATS)
                mean, var = mv[:, :, 0], mv[:, :, 1]
                rstd, shift = scales[:, 0:NT], scales[:, NT:2 * NT]
                pows.round(b)
                pows.link(pool.tensor_scalar(var_eps[:], var, EPS, None, ALU.add))
                pows.link(pool.tensor_tensor(rstd, var_eps[:], mhalf[:], ALU.pow))
                pows.step(pool.tensor_tensor(shift, mean, rstd, ALU.mult))
                pows.step(pool.tensor_tensor(var_eps[:], rstd, rstd, ALU.mult))
                pows.join_apart((setup_pool, 6))
                pows.step(pool.tensor_scalar(shift, shift, -1.0, None, ALU.mult))
                pows.step(pool.tensor_tensor(var_eps[:], var_eps[:], var, ALU.mult))
                pows.join_apart((setup_pool, 6))
                pows.link(pool.tensor_scalar(var_eps[:], var_eps[:], EPS_RMS, None, ALU.add))
                pows.step(pool.tensor_tensor(r2[:], var_eps[:], mhalf[:], ALU.pow))
                pows.end()

            def shift_difference(b, half, k):
                if k == 0:
                    pool.wait_ge(xnT_made, (b + 1) * NT)
                wait(pool, mix_made, b * 16 - 3 + k)
                pool.tensor_tensor(xx[:, k, :], xnT[:, half, k, 0:T], xnT[:, half, k, 1:T + 1],
                                   ALU.subtract).then_inc(xx_made, 1)

            def mix_lo(b, i, k):
                n = b * 16 + i * 4 + k
                pool.wait_ge(hi_made, n + 1)
                pool.tensor_tensor(mix[:, k, 1, :], mixf[:, k % 2, :], mix[:, k, 0, :].bitcast(F32),
                                   ALU.subtract).then_inc(lo_made, 1)

            def scatter(b, first, last):
                if first == 0:
                    wait_apart(pool, (setup_pool, 6), slot_made, b + 1)
                for at in range(first, last):
                    pool.indirect_dma_start(
                        d["slots"], bass.IndirectOffsetOnAxis(ap=slot[:, at:at + 1], axis=0),
                        token[:, at // TOPK:at // TOPK + 1], None, bounds_check=SLOTS - 1, oob_is_err=False,
                    ).then_inc(scattered, 16)

            def make_gate(b, m):
                pool.wait_ge(sr_made, b * 4 + m + 1)
                pool.wait_ge(sg_made, b * 4 + m + 1)
                pool.tensor_tensor(sr[:, m, :], sr[:, m, :], evac[:, m, :], ALU.mult).then_inc(gate_made, 1)

            def att_lo(b, m):
                pool.wait_ge(ah_made, b * 4 + m + 1)
                pool.tensor_tensor(att[:, m % 2, 1, :], sr[:, m, :], att[:, m % 2, 0, :].bitcast(F32),
                                   ALU.subtract).then_inc(al_made, 1)

            pool.memset(zero_tab[:], 0).then_inc(setup_pool, 1)
            pool.memset(mhalf[:], -0.5).then_inc(setup_pool, 1)
            pool.memset(ones[:], 1.0).then_inc(setup_pool, 1)
            pool.memset(seen[:], 0.0).then_inc(setup_pool, 1)
            pool.memset(a_sum[:, 0:1], 0.0).then_inc(setup_pool, 1)
            pool.memset(b_sum[:, 0:1], 0.0).then_inc(setup_pool, 1)
            pool.wait_ge(setup_pool, 6)
            norm_scales(0)
            for k in range(KC):
                shift_difference(0, 0, k)
            for k in range(KC):
                mix_lo(0, K_, k)
            pool.wait_ge(table_zeroed, 16)

            def one_round(b, half, more, before):
                mix_lo(b, V_, 0)
                if before:
                    for m in range(2):
                        make_gate(b - 1, m)
                mix_lo(b, V_, 1)
                mix_lo(b, V_, 2)
                if more:
                    norm_scales(b + 1)
                mix_lo(b, V_, 3)
                if before:
                    att_lo(b - 1, 0)
                    att_lo(b - 1, 1)
                for k in range(KC):
                    mix_lo(b, R_, k)
                scatter(b, 0, 2)
                if before:
                    att_lo(b - 1, 2)
                    att_lo(b - 1, 3)
                scatter(b, 2, 8)
                mix_lo(b, G_, 0)
                scatter(b, 8, 10)
                mix_lo(b, G_, 1)
                scatter(b, 10, 11)
                mix_lo(b, G_, 2)
                if more:
                    for k in range(KC - 1):
                        shift_difference(b + 1, 1 - half, k)
                mix_lo(b, G_, 3)
                if more:
                    mix_lo(b + 1, K_, 0)
                    shift_difference(b + 1, 1 - half, KC - 1)
                for k in range(1, KC):
                    if more:
                        mix_lo(b + 1, K_, k)
                    scatter(b, 9 + 2 * k, min(11 + 2 * k, NT * TOPK))

            rounds(pool, one_round)
            for m in range(2):
                make_gate(B - 1, m)
            for m in range(4):
                att_lo(B - 1, m)
            pool.wait_ge(scattered, 16 * B * NT * TOPK)

        @block.scalar
        def _(act):
            def make_xn(b, j):
                n = b * NT + j
                if j == 0:
                    act.wait_ge(pow_step, (b + 1) * POWS)
                act.wait_ge(x_loaded[j], (b + 1) * 16)
                wait(act, xn_turned, n - 1)
                wait(act, z_made, n - 1)
                act.activation(xn[:, j % 2, :], x_in[:, j, :], ACT.Identity, bias=scales[:, NT + j:NT + j + 1],
                               scale=scales[:, j:j + 1]).then_inc(xn_made, 1)

            def keep_turned(b, half, j):
                n = b * NT + j
                act.wait_ge(xn_turned, n + 1)
                turned = ta[:].rearrange("p (k t) -> p k t", k=KC)
                if j == 0:
                    act.activation(xnT[:, half, :, 0:1], turned[:, :, 1:2], ACT.Copy)
                act.activation(xnT[:, half, :, 1 + j * P:1 + (j + 1) * P], turned, ACT.Copy).then_inc(xnT_made, 1)
                act.wait_ge(z_turned, n + 1)
                wait(act, scores_made, n - 1)
                wait(act, zl_made, n - 1)
                wait(act, zT_stored[j % 2], (b * 2 + j // 2) * 16)
                act.activation(zT[:, j % 2, 0], tz[j % 2][:].rearrange("p (k t) -> p k t", k=KC),
                               ACT.Copy).then_inc(zh_made, 1)

            def mix_hi(b, i, k):
                n = b * 16 + i * 4 + k
                act.wait_ge(mix_made, n + 1)
                if k < KC - 1:
                    wait(act, mix_used, (b * 4 + i - 1) * 3 + k + 1)
                else:
                    wait(act, proj_done[i - 1] if i else g_done, (b + 1) * 4 if i else b * 4)
                act.activation(mix[:, k, 0, :], mixf[:, k % 2, :], ACT.Copy).then_inc(hi_made, 1)

            def exp_k(b, m):
                act.wait_ge(k_done, b * 4 + m + 1)
                wait(act, wkv_step, b * WKV - (WKV - 6 * m - 4))
                act.activation(ek[:, m, :], pj[m][:], ACT.Exp).then_inc(ek_made, 1)

            def gate_r(b, m):
                act.wait_ge(r_done, b * 4 + m + 1)
                wait(act, al_made, b * 4)
                act.activation(sr[:, m, :], pj[m][:], ACT.Sigmoid).then_inc(sr_made, 1)

            def gate_g(b, m):
                act.wait_ge(g_done, b * 4 + m + 1)
                wait(act, o_stored[m % 2], b * 32)
                act.activation(evac[:, m, :], pj[m][:], ACT.Sigmoid).then_inc(sg_made, 1)

            def route_exp(b):
                act.wait_ge(sh_made, b + 1)
                wait(act, rec_made, b)
                act.activation(ex[:], sh[:], ACT.Exp).then_inc(rexp_made, 1)

            def att_hi(b, m):
                act.wait_ge(att_made, b * 4 + m + 1)
                if m >= 2:
                    act.wait_ge(att_used, b * 3 + m - 1)
                act.activation(att[:, m % 2, 0, :], sr[:, m, :], ACT.Copy).then_inc(ah_made, 1)

            def keep_o(b, j):
                act.wait_ge(o_done, b * 4 + j + 1)
                act.wait_ge(gate_made, (b + 1) * 4)
                act.activation(evac[:, j, :], pj[j][:], ACT.Copy).then_inc(o_made, 1)

            act.wait_ge(c_loaded, 16 * 10)
            act.activation(u_mid[:], u_in[:, 0, :], ACT.Exp).then_inc(setup_act, 1)
            act.activation(first[:], u_in[:, 1, :], ACT.Exp).then_inc(setup_act, 1)
            act.wait_ge(setup_act, 2)
            act.activation(decay[:], u_mid[:], ACT.Exp, scale=-1.0).then_inc(setup_act, 1)
            act.wait_ge(setup_dve, 2)
            act.activation(wr[:, :, 0, :], wr_in[:], ACT.Copy).then_inc(setup_act, 1)
            def weight_hi(i):
                act.wait_ge(w_loaded[i], 16)
                act.activation(w[i][:, 0], stage[i], ACT.Copy).then_inc(w_hi, 1)

            make_xn(0, 0)
            make_xn(0, 1)
            weight_hi(K_)
            for j in range(NT):
                keep_turned(0, 0, j)
                if j + 2 < NT:
                    make_xn(0, j + 2)
            for k in range(KC):
                mix_hi(0, K_, k)
            weight_hi(V_)

            def one_round(b, half, more, before):
                if before:
                    route_exp(b)
                mix_hi(b, V_, 0)
                mix_hi(b, V_, 1)
                for m in range(4):
                    exp_k(b, m)
                mix_hi(b, V_, 2)
                mix_hi(b, V_, 3)
                if not before:
                    weight_hi(R_)
                    route_exp(b)
                if more:
                    make_xn(b + 1, 0)
                    make_xn(b + 1, 1)
                if before:
                    att_hi(b - 1, 0)
                    att_hi(b - 1, 1)
                for k in range(KC):
                    mix_hi(b, R_, k)
                if not before:
                    weight_hi(G_)
                if more:
                    keep_turned(b + 1, 1 - half, 0)
                if before:
                    att_hi(b - 1, 2)
                if more:
                    keep_turned(b + 1, 1 - half, 1)
                    make_xn(b + 1, 2)
                    make_xn(b + 1, 3)
                if before:
                    att_hi(b - 1, 3)
                    for j in range(NT):
                        keep_o(b - 1, j)
                if more:
                    keep_turned(b + 1, 1 - half, 2)
                    keep_turned(b + 1, 1 - half, 3)
                for k in range(KC - 1):
                    mix_hi(b, G_, k)
                for m in range(4):
                    gate_r(b, m)
                mix_hi(b, G_, 3)
                if not before:
                    weight_hi(O_)
                if more:
                    mix_hi(b + 1, K_, 0)
                    mix_hi(b + 1, K_, 1)
                if not before:
                    act.wait_ge(w_lo, 5)
                for m in range(4):
                    gate_g(b, m)
                if more:
                    mix_hi(b + 1, K_, 2)
                    mix_hi(b + 1, K_, 3)

            rounds(act, one_round)
            for m in range(4):
                att_hi(B - 1, m)
            for j in range(NT):
                keep_o(B - 1, j)

        @block.vector
        def _(dve):
            stats = Steps(dve, stats_step, STATS)
            route = Steps(dve, route_step, ROUTES)
            wkv = Steps(dve, wkv_step, WKV)

            def norm_stats(b):
                stats.round(b)
                wait(dve, pow_step, b * POWS)
                for j in range(NT):
                    dve.wait_ge(x_loaded[j], (b + 1) * 16)
                    stats.step(dve.bn_stats(st[:, j, :], x_in[:, j, :]))
                stats.join_apart((setup_pool, 6))
                for j in range(NT):
                    stats.step(dve.bn_aggr(mv[:, j, :], st[:, j, :]))
                stats.end()

            def make_z(b, j):
                n = b * NT + j
                dve.wait_ge(xn_made, n + 1)
                wait(dve, z_turned, n - 1)
                wait(dve, z_stored[j % 2], (b * 2 + j // 2) * 16)
                dve.scalar_tensor_tensor(z[:, j % 2, :], xn[:, j % 2, :], r2[:, j:j + 1], norm_w[:],
                                         ALU.mult, ALU.mult).then_inc(z_made, 1)

            def z_lo(b, j):
                n = b * NT + j
                dve.wait_ge(zh_made, n + 1)
                dve.tensor_tensor(zT[:, j % 2, 1], tz[j % 2][:].rearrange("p (k t) -> p k t", k=KC),
                                  zT[:, j % 2, 0].bitcast(F32), ALU.subtract).then_inc(zl_made, 1)

            def make_mix(b, half, i, k):
                n = b * 16 + i * 4 + k
                if i == 0:
                    dve.wait_ge(xx_made, b * 4 + k + 1)
                wait(dve, lo_made, n - 1)
                dve.scalar_tensor_tensor(mixf[:, k % 2, :], xx[:, k, :], tm[:, i, k:k + 1],
                                         xnT[:, half, k, 1:T + 1], ALU.mult, ALU.add).then_inc(mix_made, 1)

            def make_ekv(b, m):
                dve.wait_ge(v_done, b * 4 + m + 1)
                dve.wait_ge(ek_made, b * 4 + m + 1)
                wait(dve, att_made, b * 4)
                dve.tensor_tensor(ekv[:, m, :], ek[:, m, :], pj[m][:], ALU.mult).then_inc(ekv_made, 1)

            def wkv_sums(b, m):
                wkv.round(b, m * 6)
                if m == 0:
                    dve.wait_ge(ekv_made, (b + 1) * 4)
                wkv.step(dve.tensor_tensor_scan(b_sum[:, 1:T + 1], decay[:, m:m + 1].to_broadcast([P, T]), ek[:, m, :],
                                                0.0, ALU.mult, ALU.add))
                wkv.step(dve.tensor_tensor_scan(a_sum[:, 1:T + 1], decay[:, m:m + 1].to_broadcast([P, T]), ekv[:, m, :],
                                                0.0, ALU.mult, ALU.add))
                wkv.join()
                wkv.step(dve.scalar_tensor_tensor(den[:], ek[:, m, :], first[:, m:m + 1], b_sum[:, 0:T],
                                                  ALU.mult, ALU.add))
                wkv.step(dve.scalar_tensor_tensor(ekv[:, m, :], ekv[:, m, :], first[:, m:m + 1], a_sum[:, 0:T],
                                                  ALU.mult, ALU.add))

            def wkv_quotient(b, m):
                wkv.round(b, m * 6 + 4)
                wkv.join()
                wkv.link(dve.reciprocal(den[:], den[:]))
                wkv.step(dve.tensor_tensor(ekv[:, m, :], ekv[:, m, :], den[:], ALU.mult))

            def make_gate(b, m):
                dve.wait_ge(sr_made, b * 4 + m + 1)
                dve.wait_ge(sg_made, b * 4 + m + 1)
                dve.tensor_tensor(sr[:, m, :], sr[:, m, :], evac[:, m, :], ALU.mult).then_inc(gate_made, 1)

            def make_att(b, m):
                if m == 0:
                    dve.wait_ge(gate_made, (b + 1) * 4)
                    dve.wait_ge(wkv_step, (b + 1) * WKV)
                dve.tensor_tensor(sr[:, m, :], ekv[:, m, :], sr[:, m, :], ALU.mult).then_inc(att_made, 1)

            def choose(b):
                route.round(b, 0)
                dve.wait_ge(scores_made, (b + 1) * NT)
                parts = rp_lg.rearrange("p (j q e) -> p j q e", j=NT, q=2)
                dve.tensor_copy(lg[:], parts[:, :, 1, :]).then_inc(lg_low, 1)
                dve.wait_ge(lg_low, b + 1)
                dve.tensor_tensor(lg[:], lg[:], parts[:, :, 0, :], ALU.add).then_inc(lg_made, 1)
                wait_apart(dve, (setup_pool, 6), lg_made, b + 1)
                for j in range(NT):
                    route.step(dve.max(v8[:, j, :], lg[:, j, 0:E]))
                route.join_apart((setup_pool, 6))
                for j in range(NT):
                    route.step(dve.max_index(i8[:, j, :], v8[:, j, :], lg[:, j, 0:E]))
                wait(dve, rexp_made, b)
                dve.tensor_scalar(sh[:, :, E + TOPK], lg[:, :, E], -1.0, None, ALU.mult)
                dve.tensor_tensor(sh[:, :, 0:E], lg[:, :, 0:E], v8[:, :, 0:1].to_broadcast([P, NT, E]), ALU.subtract)
                dve.tensor_tensor(sh[:, :, E:E + TOPK], v8[:, :, 0:TOPK], v8[:, :, 0:1].to_broadcast([P, NT, TOPK]),
                                  ALU.subtract).then_inc(sh_made, 1)
                route.join()
                route.link(dve.tensor_copy(idxf[:].rearrange("p (j k) -> p j k", j=NT), i8[:, :, 0:TOPK]))
                route.link(dve.tensor_tensor(oh[:], idxf[:].unsqueeze(2).to_broadcast([P, NT * TOPK, E]),
                                             expert_id.unsqueeze(1).to_broadcast([P, NT * TOPK, E]), ALU.is_equal))
                wait(dve, pos_made, b)
                with nc.allow_low_precision(reason="0 or 1"):
                    route.step(dve.tensor_reduce(chosen[:], oh[:].rearrange("p (j k) e -> p j e k", j=NT), AX.X, ALU.add))
                dve.tensor_scalar(token_id, token_id, float(T), None, ALU.add)
                route.link(dve.tensor_copy(seen[:, 0, :], seen[:, NT, :]))
                for j in range(NT):
                    ins = dve.tensor_tensor(seen[:, j + 1, :], seen[:, j, :], chosen[:, j, :], ALU.add)
                    if j < NT - 1:
                        route.link(ins)
                ins.then_inc(chosen_made, 1)
                dve.wait_ge(chosen_made, b + 1)
                dve.wait_ge(pow_step, (b + 1) * POWS)
                dve.tensor_copy(keep["rec"][:, bass.ds(b * REC, 2 * NT)], scales[:]).then_inc(scales_kept, 1)

            def assign(b):
                route.round(b, CHOOSE)
                dve.wait_ge(pos_made, b + 1)
                oh4 = oh[:].rearrange("p (j k) e -> p j k e", j=NT)
                pos4 = rp_pos.rearrange("p (j e) -> p j e", j=NT).unsqueeze(2).to_broadcast([P, NT, TOPK, E])
                dve.tensor_tensor(oh4, oh4, pos4, ALU.mult).then_inc(pos_read, 1)
                dve.wait_ge(pos_read, b + 1)
                route.link(dve.tensor_reduce(pos[:], oh[:], AX.X, ALU.add))
                dve.tensor_scalar(valid[:], pos[:], float(CAP), None, ALU.is_lt)
                dve.tensor_scalar(bad[:], pos[:], float(CAP), float(DROPPED), ALU.is_ge, ALU.mult)
                route.link(dve.tensor_scalar(second[:], pos[:], float(P), float(1 - P * ROW), ALU.is_ge, ALU.mult))
                dve.scalar_tensor_tensor(s1[:], idxf[:], float(NCT), bad[:], ALU.mult, ALU.add)
                route.link(dve.scalar_tensor_tensor(s2[:], pos[:], float(ROW), second[:], ALU.mult, ALU.add))
                wait(dve, scattered, b * NT * TOPK * 16)
                dve.tensor_copy(token[:], token_id)
                dve.tensor_tensor(slot[:], s1[:], s2[:], ALU.add).then_inc(slot_made, 1)
                dve.wait_ge(rexp_made, b + 1)
                dve.tensor_scalar(tot[:, :, 1], ex[:, :, E + TOPK], 1.0, None, ALU.add)
                route.link(dve.tensor_reduce(tot[:, :, 0], ex[:, :, 0:E], AX.X, ALU.add))
                route.link(dve.reciprocal(rtot[:], tot[:]))
                weight = rec[:, 0:NT * TOPK]
                route.link(dve.tensor_tensor(weight.rearrange("p (j k) -> p j k", j=NT), ex[:, :, E:E + TOPK],
                                             rtot[:, :, 0:1].to_broadcast([P, NT, TOPK]), ALU.mult))
                dve.tensor_copy(rec[:, NT * TOPK:], rtot[:, :, 1])
                route.link(dve.tensor_tensor(weight, weight, valid[:], ALU.mult))
                dve.wait_ge(slot_made, b + 1)
                dve.tensor_copy(keep["slot"][:, bass.ds(b * NT * TOPK, NT * TOPK)], slot[:])
                dve.tensor_copy(keep["rec"][:, bass.ds(b * REC + 2 * NT, REC - 2 * NT)], rec[:]).then_inc(rec_made, 1)
                route.end()

            dve.wait_ge(setup_pool, 6)
            norm_stats(0)
            dve.wait_ge(c_loaded, 16 * 10)
            dve.tensor_copy(before[:], before_in).then_inc(setup_dve, 1)
            dve.memset(wr_in[:, :, RW - 1:RW], 0.0).then_inc(setup_dve, 1)
            dve.wait_ge(setup_act, 4)
            dve.tensor_tensor(wr[:, :, 1, :], wr_in[:], wr[:, :, 0, :].bitcast(F32), ALU.subtract).then_inc(setup_dve, 1)
            dve.wait_ge(setup_pool, 6)

            def weight_lo(i):
                dve.wait_ge(w_hi, i + 1)
                dve.tensor_tensor(w[i][:, 1], stage[i], w[i][:, 0].bitcast(F32), ALU.subtract).then_inc(w_lo, 1)

            make_z(0, 0)
            make_z(0, 1)
            weight_lo(K_)
            for j in range(NT):
                z_lo(0, j)
                if j + 2 < NT:
                    make_z(0, j + 2)
            for k in range(KC):
                make_mix(0, 0, K_, k)
            weight_lo(V_)

            def one_round(b, half, more, before):
                make_mix(b, half, V_, 0)
                make_mix(b, half, V_, 1)
                if more:
                    norm_stats(b + 1)
                make_mix(b, half, V_, 2)
                if before:
                    assign(b)
                make_mix(b, half, V_, 3)
                if before:
                    for m in range(2, 4):
                        make_gate(b - 1, m)
                    for m in range(4):
                        make_att(b - 1, m)
                if not before:
                    weight_lo(R_)
                    choose(b)
                make_mix(b, half, R_, 0)
                if more:
                    make_z(b + 1, 0)
                    make_z(b + 1, 1)
                make_mix(b, half, R_, 1)
                make_mix(b, half, R_, 2)
                for m in range(4):
                    make_ekv(b, m)
                make_mix(b, half, R_, 3)
                if more:
                    z_lo(b + 1, 0)
                    z_lo(b + 1, 1)
                if not before:
                    weight_lo(G_)
                    assign(b)
                wkv_sums(b, 0)
                wkv_quotient(b, 0)
                if more:
                    make_z(b + 1, 2)
                    make_z(b + 1, 3)
                make_mix(b, half, G_, 0)
                wkv_sums(b, 1)
                make_mix(b, half, G_, 1)
                wkv_quotient(b, 1)
                if more:
                    z_lo(b + 1, 2)
                    z_lo(b + 1, 3)
                wkv_sums(b, 2)
                make_mix(b, half, G_, 2)
                wkv_quotient(b, 2)
                make_mix(b, half, G_, 3)
                if not before:
                    weight_lo(O_)
                if more:
                    choose(b + 1)
                if more:
                    make_mix(b + 1, 1 - half, K_, 0)
                if more:
                    make_mix(b + 1, 1 - half, K_, 1)
                wkv_sums(b, 3)
                if more:
                    make_mix(b + 1, 1 - half, K_, 2)
                wkv_quotient(b, 3)
                if more:
                    make_mix(b + 1, 1 - half, K_, 3)

            rounds(dve, one_round)
            for m in range(2, 4):
                make_gate(B - 1, m)
            for m in range(4):
                make_att(B - 1, m)

        @block.tensor
        def _(pe):
            def turn(b, j, src, dst, made, free, done, back):
                n = b * NT + j
                pe.wait_ge(made, n + 1)
                wait(pe, free, n - back)
                for k in range(KC):
                    last = pe.transpose(dst[:, k * P:(k + 1) * P],
                                        src[:, j % 2, :].rearrange("p (c k) -> p k c", k=KC)[:, k, :], ident)
                last.then_inc(done, 1)

            def turn_z(b, j):
                turn(b, j, z, tz[j % 2], z_made, zl_made, z_turned, 1)

            def turn_xn(b, j):
                turn(b, j, xn, ta, xn_made, xnT_made, xn_turned, 0)

            def score(b, j):
                n = b * NT + j
                pe.wait_ge(zl_made, n + 1)
                if j == 0:
                    wait(pe, pos_read, b)
                for x_part in (1, 0):
                    for k in range(KC):
                        last = pe.matmul(rp_lg[:, j * 2 * RW:(j + 1) * 2 * RW], zT[:, j % 2, x_part, k, :],
                                         wr[:, k].rearrange("p q e -> p (q e)"),
                                         start=(x_part == 1 and k == 0), stop=(x_part == 0 and k == KC - 1))
                last.then_inc(scores_made, 1)

            def count(b):
                pe.wait_ge(chosen_made, b + 1)
                wait(pe, pos_read, b)
                pe.matmul(rp_pos, before[:], chosen[:].rearrange("p j e -> p (j e)"), start=True, stop=False)
                pe.matmul(rp_pos, ones[:], seen[:, 0:NT, :].rearrange("p j e -> p (j e)"),
                          start=False, stop=True).then_inc(pos_made, 1)

            def taken(b, i, m):
                if i == K_:
                    wait(pe, sg_made, b * 4 - 3 + m if not isinstance(b, int) or b else 0)
                elif i == R_:
                    if isinstance(b, int) and b == 0:
                        pe.wait_ge(ekv_made, m + 1)
                    else:
                        pe.wait_ge(o_made, b * 4 - 3 + m)
                else:
                    pe.wait_ge(ek_made if i == V_ else sr_made, b * 4 + m + 1)

            def project(b, i):
                if isinstance(b, int) and b == 0:
                    pe.wait_ge(w_lo, i + 1)
                for k in range(KC):
                    n = b * 16 + i * 4 + k
                    pe.wait_ge(lo_made, n + 1)
                    for m in range(4):
                        if k == 0:
                            taken(b, i, m)
                        for q, (w_part, x_part) in enumerate(PRODUCTS):
                            last = pe.matmul(pj[m][:], w[i][:, w_part, k, m * P:(m + 1) * P], mix[:, k, x_part, :],
                                             start=(k == 0 and q == 0), stop=(k == KC - 1 and q == 2))
                        if k == KC - 1:
                            last.then_inc(proj_done[i], 1)
                    if k < KC - 1:
                        last.then_inc(mix_used, 1)

            def project_out(b, m, bank_taken):
                pe.wait_ge(al_made, b * 4 + m + 1)
                for j in range(NT):
                    if m == 0:
                        bank_taken(j)
                    for q, (x_part, w_part) in enumerate(PRODUCTS):
                        last = pe.matmul(pj[j][:], att[:, m % 2, x_part, j * P:(j + 1) * P], w[O_][:, w_part, m, :],
                                         start=(m == 0 and q == 0), stop=(m == 3 and q == 2))
                    if m == 3:
                        last.then_inc(o_done, 1)
                if m < 3:
                    last.then_inc(att_used, 1)

            pe.wait_ge(setup_dve, 3)
            for j in range(NT):
                turn_z(0, j)
                turn_xn(0, j)
                if j:
                    score(0, j - 1)
            score(0, NT - 1)

            def one_round(b, half, more, before):
                project(b, K_)
                project(b, V_)
                if not before:
                    count(b)
                if more:
                    turn_z(b + 1, 0)
                    turn_xn(b + 1, 0)
                    turn_z(b + 1, 1)
                for m in range(4):
                    if before:
                        project_out(b - 1, m, lambda j: pe.wait_ge(ekv_made, b * 4 + j + 1))
                    if more and m == 0:
                        turn_xn(b + 1, 1)
                if more:
                    for j in (0, 1):
                        score(b + 1, j)
                        turn_z(b + 1, j + 2)
                        turn_xn(b + 1, j + 2)
                project(b, R_)
                if more:
                    score(b + 1, 2)
                    score(b + 1, 3)
                project(b, G_)
                if more:
                    count(b + 1)
                if not before:
                    pe.wait_ge(w_lo, 5)

            rounds(pe, one_round)
            for m in range(4):
                project_out(B - 1, m, lambda j: pe.wait_ge(sg_made, (B - 1) * 4 + j + 1))


def expert_stage(nc, keep, d):
    with ExitStack() as ctx:
        def sb(name, shape, dt=F32):
            return ctx.enter_context(nc.sbuf_tensor(name, shape, dt))

        def sem(name):
            return ctx.enter_context(nc.semaphore(name))

        ident = sb("e_ident", [P, P])
        table = sb("e_table", [P, ROW], U32)
        index = sb("e_index", [P, 2, NCT, 1], U32)
        g_in = sb("e_g_in", [P, 2, KC * F])
        u_in = sb("e_u_in", [P, 2, KC * F])
        d_in = sb("e_d_in", [P, 2, len(FT), C])
        wg = sb("e_wg", [P, 2, 2, KC * F], F32R)
        wu = sb("e_wu", [P, 2, 2, KC * F], F32R)
        wd = sb("e_wd", [P, 2, 2, len(FT), C], F32R)
        rows = sb("e_rows", [P, 2, NCT, C])
        xT = sb("e_xT", [P, 2, 2, KC, CAP], F32R)
        act_g = sb("e_act_g", [P, len(FT), CAP])
        h = sb("e_h", [P, len(FT), 2, CAP], F32R)
        y = sb("e_y", [P, 2, NCT, C])

        xt = [ctx.enter_context(nc.psum_tensor(f"e_xt{i}", [P, 512], F32)) for i in range(2)]
        gu = [ctx.enter_context(nc.psum_tensor(f"e_gu{i}", [P, 2, CAP], F32)) for i in range(len(FT))]
        yp = [ctx.enter_context(nc.psum_tensor(f"e_yp{i}", [P, C], F32)) for i in range(NCT)]

        table_loaded, ident_loaded = sem("e_table_loaded"), sem("e_ident_loaded")
        g_loaded, u_loaded, d_loaded = ([sem(f"e_{n}_loaded{i}") for i in range(2)] for n in "gud")
        index_made = sem("e_index_made")
        gathered = [sem(f"e_gathered{i}") for i in range(2)]
        turned = sem("e_turned")
        x_hi, x_lo = sem("e_x_hi"), sem("e_x_lo")
        wg_hi, wu_hi, wd_hi = sem("e_wg_hi"), sem("e_wu_hi"), sem("e_wd_hi")
        wg_lo, wu_lo, wd_lo = sem("e_wg_lo"), sem("e_wu_lo"), sem("e_wd_lo")
        up_done, silu_made = sem("e_up_done"), sem("e_silu_made")
        h_made, h_hi, h_lo = sem("e_h_made"), sem("e_h_hi"), sem("e_h_lo")
        y_done, y_made = sem("e_y_done"), sem("e_y_made")
        y_stored = [sem(f"e_y_stored{i}") for i in range(2)]

        NF = len(FT)
        block = ctx.enter_context(nc.Block())

        def experts(eng, one_expert):
            one_expert(0, 0, 2, 1)
            with eng.Fori(0, E // 2 - 2) as r:
                one_expert(r * 2 + 1, 1, 2, r + 1)
                one_expert(r * 2 + 2, 0, 2, r + 2)
            one_expert(E - 3, 1, 2, E // 2 - 1)
            one_expert(E - 2, 0, 1, E // 2)
            one_expert(E - 1, 1, 0, E // 2)

        @block.sync
        def _(sp):
            def load(e, half):
                wait(sp, wg_lo, e - 1)
                sp.dma_start(g_in[:, half, :], d["w_gate"](e)).then_inc(g_loaded[half], 16)
                wait(sp, wu_lo, e - 1)
                sp.dma_start(u_in[:, half, :], d["w_up"](e)).then_inc(u_loaded[half], 16)
                wait(sp, wd_lo, e - 1)
                sp.dma_start(d_in[:, half, 0:NF - 1, :], d["w_down_a"](e)).then_inc(d_loaded[half], 16)
                sp.dma_start(d_in[0:FT[-1][1], half, NF - 1, :], d["w_down_b"](e)).then_inc(d_loaded[half], 16)

            def one_expert(e, half, more, uses):
                if more == 2:
                    load(e + 2, half)
                sp.wait_ge(y_made, (e + 1) * NCT)
                sp.dma_start(d["y_rows"](e), y[:, half].rearrange("p c n -> p (c n)")).then_inc(y_stored[half], 16)

            sp.dma_start(table[:], d["table"]).then_inc(table_loaded, 16)
            sp.dma_start(ident[:], d["const"][:, 0:P]).then_inc(ident_loaded, 16)
            load(0, 0)
            sp.wait_ge(gathered[0], 32)
            load(1, 1)
            experts(sp, one_expert)
            for i in range(2):
                sp.wait_ge(y_stored[i], 16 * E // 2)

        @block.gpsimd
        def _(pool):
            def gather(e, half):
                wait(pool, turned, e - 1)
                wait_apart(pool, (table_loaded, 16), index_made, e + 1)
                for c in range(NCT):
                    pool.indirect_dma_start(
                        rows[:, half, c, :], None, d["z_rows"],
                        bass.IndirectOffsetOnAxis(ap=index[:, half, c, :], axis=0),
                    ).then_inc(gathered[half], 16)

            def gate_lo(e, half):
                pool.wait_ge(wg_hi, e + 1)
                pool.tensor_tensor(wg[:, half, 1, :], g_in[:, half, :], wg[:, half, 0, :].bitcast(F32),
                                   ALU.subtract).then_inc(wg_lo, 1)

            gather(0, 0)
            gather(1, 1)
            gate_lo(0, 0)

            def one_expert(e, half, more, uses):
                if more:
                    gate_lo(e + 1, 1 - half)
                if more == 2:
                    gather(e + 2, half)

            experts(pool, one_expert)

        @block.scalar
        def _(act):
            def gate_hi(e, half, uses):
                act.wait_ge(g_loaded[half], uses * 16)
                wait(act, y_done, (e - 1) * NCT)
                act.activation(wg[:, half, 0, :], g_in[:, half, :], ACT.Copy).then_inc(wg_hi, 1)

            def up_hi(e, half, uses):
                act.wait_ge(u_loaded[half], uses * 16)
                act.activation(wu[:, half, 0, :], u_in[:, half, :], ACT.Copy).then_inc(wu_hi, 1)

            def down_hi(e, half, uses):
                act.wait_ge(d_loaded[half], uses * 32)
                act.activation(wd[:, half, 0, 0:NF - 1, :], d_in[:, half, 0:NF - 1, :], ACT.Copy)
                m = FT[-1][1]
                act.activation(wd[0:m, half, 0, NF - 1, :], d_in[0:m, half, NF - 1, :], ACT.Copy).then_inc(wd_hi, 1)

            def rows_hi(e, half):
                act.wait_ge(turned, e + 1)
                for i in range(2):
                    act.activation(xT[:, half, 0, 2 * i:2 * i + 2, :],
                                   xt[i][:].rearrange("p (k s) -> p k s", k=2), ACT.Copy).then_inc(x_hi, 1)

            def silu(e, f):
                m = FT[f][1]
                act.wait_ge(up_done, e * NF + f + 1)
                wait(act, h_lo, (e - 1) * NF + f + 1)
                act.activation(act_g[0:m, f, :], gu[f][0:m, 0, :], ACT.Silu).then_inc(silu_made, 1)

            def hidden_hi(e, f):
                m = FT[f][1]
                act.wait_ge(h_made, e * NF + f + 1)
                wait(act, y_done, e * NCT)
                act.activation(h[0:m, f, 0, :], act_g[0:m, f, :], ACT.Copy).then_inc(h_hi, 1)

            def keep_y(e, half, uses):
                for c in range(NCT):
                    act.wait_ge(y_done, e * NCT + c + 1)
                    if c == 0:
                        wait(act, y_stored[half], (uses - 1) * 16)
                    act.activation(y[:, half, c, :], yp[c][:], ACT.Copy).then_inc(y_made, 1)

            gate_hi(0, 0, 1)
            up_hi(0, 0, 1)
            down_hi(0, 0, 1)
            rows_hi(0, 0)

            def one_expert(e, half, more, uses):
                other = uses + half
                if more:
                    gate_hi(e + 1, 1 - half, other)
                silu(e, 0)
                if more:
                    up_hi(e + 1, 1 - half, other)
                hidden_hi(e, 0)
                silu(e, 1)
                hidden_hi(e, 1)
                silu(e, 2)
                if more:
                    rows_hi(e + 1, 1 - half)
                hidden_hi(e, 2)
                if more:
                    down_hi(e + 1, 1 - half, other)
                keep_y(e, half, uses)

            experts(act, one_expert)

        @block.vector
        def _(dve):
            def make_index(e, half, uses):
                wait(dve, gathered[half], (uses - 1) * 32)
                dve.tensor_copy(index[:, half, :, 0], table[:, bass.ds(e * NCT, NCT)]).then_inc(index_made, 1)

            def up_lo(e, half):
                dve.wait_ge(wu_hi, e + 1)
                dve.tensor_tensor(wu[:, half, 1, :], u_in[:, half, :], wu[:, half, 0, :].bitcast(F32),
                                  ALU.subtract).then_inc(wu_lo, 1)

            def down_lo(e, half):
                dve.wait_ge(wd_hi, e + 1)
                m = FT[-1][1]
                dve.tensor_tensor(wd[:, half, 1, 0:NF - 1, :], d_in[:, half, 0:NF - 1, :],
                                  wd[:, half, 0, 0:NF - 1, :].bitcast(F32), ALU.subtract)
                dve.tensor_tensor(wd[0:m, half, 1, NF - 1, :], d_in[0:m, half, NF - 1, :],
                                  wd[0:m, half, 0, NF - 1, :].bitcast(F32), ALU.subtract).then_inc(wd_lo, 1)

            def rows_lo(e, half):
                for i in range(2):
                    dve.wait_ge(x_hi, e * 2 + i + 1)
                    dve.tensor_tensor(xT[:, half, 1, 2 * i:2 * i + 2, :], xt[i][:].rearrange("p (k s) -> p k s", k=2),
                                      xT[:, half, 0, 2 * i:2 * i + 2, :].bitcast(F32), ALU.subtract).then_inc(x_lo, 1)

            def hidden(e, f):
                m = FT[f][1]
                dve.wait_ge(silu_made, e * NF + f + 1)
                dve.tensor_tensor(act_g[0:m, f, :], act_g[0:m, f, :], gu[f][0:m, 1, :], ALU.mult).then_inc(h_made, 1)

            def hidden_lo(e, f):
                m = FT[f][1]
                dve.wait_ge(h_hi, e * NF + f + 1)
                dve.tensor_tensor(h[0:m, f, 1, :], act_g[0:m, f, :], h[0:m, f, 0, :].bitcast(F32),
                                  ALU.subtract).then_inc(h_lo, 1)

            dve.wait_ge(table_loaded, 16)
            make_index(0, 0, 1)
            make_index(1, 1, 1)
            up_lo(0, 0)
            down_lo(0, 0)
            rows_lo(0, 0)

            def one_expert(e, half, more, uses):
                if more == 2:
                    make_index(e + 2, half, uses + 1)
                hidden(e, 0)
                if more:
                    up_lo(e + 1, 1 - half)
                hidden_lo(e, 0)
                hidden(e, 1)
                hidden_lo(e, 1)
                hidden(e, 2)
                if more:
                    rows_lo(e + 1, 1 - half)
                hidden_lo(e, 2)
                if more:
                    down_lo(e + 1, 1 - half)

            experts(dve, one_expert)

        @block.tensor
        def _(pe):
            def turn(e, half, uses):
                pe.wait_ge(gathered[half], uses * 32)
                wait(pe, x_lo, e * 2)
                for c in range(NCT):
                    for k in range(KC):
                        last = pe.transpose(xt[k // 2][:, (k % 2) * CAP + c * P:(k % 2) * CAP + (c + 1) * P],
                                            rows[:, half, c, :].rearrange("p (n k) -> p k n", k=KC)[:, k, :], ident[:])
                last.then_inc(turned, 1)

            def product(e, half, f, which, w):
                f0, m = FT[f]
                for q, (w_part, x_part) in enumerate(PRODUCTS):
                    for k in range(KC):
                        last = pe.matmul(gu[f][0:m, which, :], w[:, half, w_part, k * F + f0:k * F + f0 + m],
                                         xT[:, half, x_part, k, :], start=(q == 0 and k == 0),
                                         stop=(q == 2 and k == KC - 1))
                return last

            def up_gate(e, half, f):
                if f == 0:
                    pe.wait_ge(x_lo, (e + 1) * 2)
                    pe.wait_ge(wg_lo, e + 1)
                wait(pe, h_made, (e - 1) * NF + f + 1)
                product(e, half, f, 0, wg)
                if f == 0:
                    pe.wait_ge(wu_lo, e + 1)
                product(e, half, f, 1, wu).then_inc(up_done, 1)

            def down(e, half):
                wait(pe, y_made, e * NCT)
                pe.wait_ge(wd_lo, e + 1)
                for f in range(NF):
                    m = FT[f][1]
                    pe.wait_ge(h_lo, e * NF + f + 1)
                    for c in range(NCT):
                        for q, (h_part, w_part) in enumerate(PRODUCTS):
                            last = pe.matmul(yp[c][:], h[0:m, f, h_part, c * P:(c + 1) * P], wd[0:m, half, w_part, f, :],
                                             start=(f == 0 and q == 0), stop=(f == NF - 1 and q == 2))
                        if f == NF - 1:
                            last.then_inc(y_done, 1)

            pe.wait_ge(ident_loaded, 16)
            turn(0, 0, 1)

            def one_expert(e, half, more, uses):
                for f in range(NF):
                    up_gate(e, half, f)
                if more:
                    turn(e + 1, 1 - half, uses + half)
                down(e, half)

            experts(pe, one_expert)


def output_stage(nc, keep, d):
    with ExitStack() as ctx:
        def sb(name, shape, dt=F32):
            return ctx.enter_context(nc.sbuf_tensor(name, shape, dt))

        def sem(name):
            return ctx.enter_context(nc.semaphore(name))

        wg = sb("s_wg", [P, 2, KC, FS], F32R)
        wu = sb("s_wu", [P, 2, KC, FS], F32R)
        wd = sb("s_wd", [P, 2, NFS, C], F32R)
        with nc.sbuf_tensor("s_piece", [P, 2, 3, C], F32) as both:
            piece = [both[:, i] for i in range(2)]
        zT = [sb(f"s_zT{i}", [P, NT, 2, KC, P], F32R) for i in (1, 0)][::-1]
        act_g = sb("s_act_g", [P, 2, T])
        h = sb("s_h", [P, 2, 2, T], F32R)
        total = sb("s_total", [P, NT, C])
        picked = sb("s_picked", [P, TOPK, C])
        x = sb("s_x", [P, C])
        o = sb("s_o", [P, C])
        xn = sb("s_xn", [P, C])
        ln_g = sb("s_ln_g", [P, C])
        ln_b = sb("s_ln_b", [P, C])
        rec = sb("s_rec", [P, REC])
        slot = sb("s_slot", [P, NT * TOPK], U32)
        st = sb("s_st", [P, 6])
        mv = sb("s_mv", [P, 2])
        o_var = sb("s_o_var", [P, 1])
        o_rstd = sb("s_o_rstd", [P, 1])
        mhalf = sb("s_mhalf", [P, 1])

        gp = [ctx.enter_context(nc.psum_tensor(f"s_gp{i}", [P, T], F32)) for i in range(2)]
        up = [ctx.enter_context(nc.psum_tensor(f"s_up{i}", [P, T], F32)) for i in range(2)]
        yp = [ctx.enter_context(nc.psum_tensor(f"s_yp{j}", [P, C], F32)) for j in range(NT)]

        c_loaded, setup = sem("s_c_loaded"), sem("s_setup")
        piece_loaded = [sem(f"s_piece_loaded{i}") for i in range(2)]
        w_hi, w_lo = sem("s_w_hi"), sem("s_w_lo")
        zT_loaded = [sem(f"s_zT_loaded{i}") for i in range(2)]
        gate_done, up_done, silu_made = sem("s_gate_done"), sem("s_up_done"), sem("s_silu_made")
        h_made, h_hi, h_lo = sem("s_h_made"), sem("s_h_hi"), sem("s_h_lo")
        h_used, y_done = sem("s_h_used"), sem("s_y_done")
        x_loaded, o_loaded = sem("s_x_loaded"), sem("s_o_loaded")
        slot_made, rec_made = sem("s_slot_made"), sem("s_rec_made")
        gathered = [sem(f"s_gathered{k}") for k in range(TOPK)]
        picked_used = sem("s_picked_used")
        xn_made, base_step, stats_step, rstd_step = (sem("s_xn_made"), sem("s_base_step"), sem("s_stats_step"),
                                                     sem("s_rstd_step"))
        sum_step, total_made, out_stored = sem("s_sum_step"), sem("s_total_made"), [sem(f"s_out_stored{j}") for j in range(NT)]

        block = ctx.enter_context(nc.Block())

        def rounds(eng, one_round):
            one_round(0, 0, True, 0)
            with eng.Fori(0, B // 2 - 1) as r:
                one_round(r * 2 + 1, 1, True, r)
                one_round(r * 2 + 2, 0, True, r + 1)
            one_round(B - 1, 1, False, B // 2 - 1)

        def chunk(t, f):
            return t[:, :, f * P:(f + 1) * P]

        @block.sync
        def _(sp):
            def load_zT(b, half):
                wait(sp, up_done, (b - 1) * NFS)
                for j in range(NT):
                    sp.dma_start(zT[half][:, j].bitcast(F32), d["zT_tile"](b, j)).then_inc(zT_loaded[half], 16)

            def load_xo(b, j):
                n = b * NT + j
                wait(sp, base_step, n * 2)
                sp.dma_start(x[:], d["x_tile"](b, j)).then_inc(x_loaded, 16)
                wait(sp, sum_step, n * 2)
                sp.dma_start(o[:], d["o_tile"](b, j)).then_inc(o_loaded, 16)

            def store(b, j):
                wait_apart(sp, (c_loaded, 32), total_made, b * NT + j + 1)
                sp.dma_start(d["out_tile"](b, j), total[:, j, :]).then_inc(out_stored[j], 16)

            def load_piece(f):
                wait(sp, w_lo, f - 1)
                i = f % 2
                sp.dma_start(piece[i][:, 0, :].rearrange("p (k f) -> p k f", k=KC),
                             chunk(d["sw_gate"].rearrange("(p k) f -> p k f", k=KC), f)).then_inc(piece_loaded[i], 16)
                sp.dma_start(piece[i][:, 1, :].rearrange("p (k f) -> p k f", k=KC),
                             chunk(d["sw_up"].rearrange("(p k) f -> p k f", k=KC), f)).then_inc(piece_loaded[i], 16)
                sp.dma_start(piece[i][:, 2, :], d["sw_down"][f * P:(f + 1) * P, :]).then_inc(piece_loaded[i], 16)

            load_piece(0)
            load_zT(0, 0)
            load_piece(1)
            sp.dma_start(ln_g[:], d["ln_g"].rearrange("(o c) -> o c", o=1).to_broadcast([P, C])).then_inc(c_loaded, 16)
            sp.dma_start(ln_b[:], d["ln_b"].rearrange("(o c) -> o c", o=1).to_broadcast([P, C])).then_inc(c_loaded, 16)
            load_xo(0, 0)

            def one_round(b, half, more, r):
                first = isinstance(b, int) and b == 0
                if first:
                    for f in range(2, 5):
                        load_piece(f)
                elif more:
                    load_zT(b + 1, 1 - half)
                for j in range(1, NT):
                    load_xo(b, j)
                    if first:
                        load_piece(2 * j + 3)
                        load_piece(2 * j + 4)
                if first:
                    sp.wait_ge(w_lo, NFS)
                    load_zT(1, 1)
                if more:
                    load_xo(b + 1, 0)
                for j in range(NT):
                    store(b, j)

            rounds(sp, one_round)
            for j in range(NT):
                sp.wait_ge(out_stored[j], 16 * B)

        @block.gpsimd
        def _(pool):
            base = Steps(pool, base_step, 2)
            rstd = Steps(pool, rstd_step, 2)

            def gather(b, j):
                n = b * NT + j
                if j == 0:
                    pool.wait_ge(slot_made, b + 1)
                for k in range(TOPK):
                    wait_apart(pool, (setup, 2), picked_used, (n - 1) * TOPK + k + 1)
                    pool.indirect_dma_start(
                        picked[:, k, :], None, d["y_flat"],
                        bass.IndirectOffsetOnAxis(ap=slot[:, j * TOPK + k:j * TOPK + k + 1], axis=0),
                        bounds_check=SLOTS - 1, oob_is_err=False,
                    ).then_inc(gathered[k], 16)

            def add_base(b, j):
                n = b * NT + j
                base.round(n)
                pool.wait_ge(xn_made, n + 1)
                wait(pool, out_stored[j], b * 16)
                base.link(pool.tensor_tensor(total[:, j, :], xn[:], x[:], ALU.add))
                base.step(pool.tensor_tensor(total[:, j, :], total[:, j, :], ln_b[:], ALU.add))

            def attention_rstd(b, j):
                n = b * NT + j
                rstd.round(n)
                wait_apart(pool, (setup, 2), stats_step, (n + 1) * 2)
                wait(pool, sum_step, n * 2)
                rstd.link(pool.tensor_scalar(o_var[:], mv[:, 1:2], EPS, None, ALU.add))
                rstd.step(pool.tensor_tensor(o_rstd[:], o_var[:], mhalf[:], ALU.pow))

            pool.memset(mhalf[:], -0.5).then_inc(setup, 1)
            pool.wait_ge(setup, 1)
            pool.memset(picked[:], 0.0).then_inc(setup, 1)
            pool.wait_ge(setup, 2)
            pool.wait_ge(c_loaded, 32)
            gather(0, 0)

            def one_round(b, half, more, r):
                for j in range(NT):
                    add_base(b, j)
                    attention_rstd(b, j)
                    if j + 1 < NT:
                        gather(b, j + 1)
                    elif more:
                        gather(b + 1, 0)

            rounds(pool, one_round)

        @block.scalar
        def _(act):
            def silu(b, half, f):
                n = b * NFS + f
                i = (half * NFS + f) % 2
                act.wait_ge(gate_done, n + 1)
                wait(act, h_lo, n - 1)
                act.activation(act_g[:, i, :], gp[i][:], ACT.Silu).then_inc(silu_made, 1)

            def hidden_hi(b, half, f):
                n = b * NFS + f
                i = (half * NFS + f) % 2
                act.wait_ge(h_made, n + 1)
                if f == 1:
                    wait(act, y_done, b * NT)
                else:
                    wait(act, h_used, b * (NFS - 1) + max(f - 1, 0))
                act.activation(h[:, i, 0, :], act_g[:, i, :], ACT.Copy).then_inc(h_hi, 1)

            def make_xn(b, j):
                n = b * NT + j
                if j == 0:
                    act.wait_ge(rec_made, b + 1)
                act.wait_ge(x_loaded, (n + 1) * 16)
                wait(act, base_step, n * 2)
                act.activation(xn[:], x[:], ACT.Identity, bias=rec[:, NT + j:NT + j + 1],
                               scale=rec[:, j:j + 1]).then_inc(xn_made, 1)

            def piece_hi(f):
                i = f % 2
                act.wait_ge(piece_loaded[i], (f // 2 + 1) * 48)
                act.activation(chunk(wg[:, 0], f), piece[i][:, 0, :].rearrange("p (k f) -> p k f", k=KC), ACT.Copy)
                act.activation(chunk(wu[:, 0], f), piece[i][:, 1, :].rearrange("p (k f) -> p k f", k=KC), ACT.Copy)
                act.activation(wd[:, 0, f, :], piece[i][:, 2, :], ACT.Copy).then_inc(w_hi, 1)

            piece_hi(0)
            piece_hi(1)
            silu(0, 0, 0)

            def one_round(b, half, more, r):
                for f in range(NFS):
                    hidden_hi(b, half, f)
                    if f + 1 < NFS:
                        silu(b, half, f + 1)
                    elif more:
                        silu(b + 1, 1 - half, 0)
                    if isinstance(b, int) and b == 0 and f + 2 < NFS:
                        piece_hi(f + 2)
                    if f % 2 == 0 and f < 2 * NT:
                        make_xn(b, f // 2)

            rounds(act, one_round)

        @block.vector
        def _(dve):
            stats = Steps(dve, stats_step, 2)
            sums = Steps(dve, sum_step, 2)

            def hidden(b, half, f):
                n = b * NFS + f
                i = (half * NFS + f) % 2
                dve.wait_ge(silu_made, n + 1)
                dve.wait_ge(up_done, n + 1)
                dve.tensor_tensor(act_g[:, i, :], act_g[:, i, :], up[i][:], ALU.mult).then_inc(h_made, 1)

            def hidden_lo(b, half, f):
                n = b * NFS + f
                i = (half * NFS + f) % 2
                dve.wait_ge(h_hi, n + 1)
                dve.tensor_tensor(h[:, i, 1, :], act_g[:, i, :], h[:, i, 0, :].bitcast(F32),
                                  ALU.subtract).then_inc(h_lo, 1)

            def fetch_rec(b):
                wait(dve, total_made, b * NT)
                dve.tensor_copy(rec[:], keep["rec"][:, bass.ds(b * REC, REC)]).then_inc(rec_made, 1)
                for k in range(TOPK):
                    wait(dve, gathered[k], b * NT * 16)
                dve.tensor_copy(slot[:], keep["slot"][:, bass.ds(b * NT * TOPK, NT * TOPK)]).then_inc(slot_made, 1)

            def attention_stats(b, j):
                n = b * NT + j
                stats.round(n)
                dve.wait_ge(o_loaded, (n + 1) * 16)
                wait(dve, rstd_step, n * 2)
                stats.step(dve.bn_stats(st[:], o[:]))
                stats.join_apart((setup, 1))
                stats.step(dve.bn_aggr(mv[:], st[:]))

            def add_attention(b, j):
                n = b * NT + j
                sums.round(n)
                dve.wait_ge(stats_step, (n + 1) * 2)
                sums.link(dve.scalar_tensor_tensor(o[:], o[:], mv[:, 0:1], ln_g[:], ALU.subtract, ALU.mult))
                dve.wait_ge(rstd_step, (n + 1) * 2)
                dve.wait_ge(base_step, (n + 1) * 2)
                sums.link(dve.scalar_tensor_tensor(total[:, j, :], o[:], o_rstd[:, 0:1], total[:, j, :],
                                                   ALU.mult, ALU.add))

            def add_expert(b, j, k):
                n = b * NT + j
                dve.wait_ge(gathered[k], (n + 1) * 16)
                if k:
                    dve.wait_ge(picked_used, n * TOPK + k)
                at = 2 * NT + j * TOPK + k
                dve.scalar_tensor_tensor(total[:, j, :], picked[:, k, :], rec[:, at:at + 1], total[:, j, :],
                                         ALU.mult, ALU.add).then_inc(picked_used, 1)

            def finish(b, j):
                dve.wait_ge(y_done, b * NT + j + 1)
                dve.wait_ge(picked_used, (b * NT + j + 1) * TOPK)
                dve.scalar_tensor_tensor(total[:, j, :], yp[j][:], rec[:, REC - NT + j:REC - NT + j + 1], total[:, j, :],
                                         ALU.mult, ALU.add).then_inc(total_made, 1)

            dve.wait_ge(setup, 1)
            fetch_rec(0)
            def piece_lo(f):
                i = f % 2
                dve.wait_ge(w_hi, f + 1)
                dve.tensor_tensor(chunk(wg[:, 1], f), piece[i][:, 0, :].rearrange("p (k f) -> p k f", k=KC),
                                  chunk(wg[:, 0], f).bitcast(F32), ALU.subtract)
                dve.tensor_tensor(chunk(wu[:, 1], f), piece[i][:, 1, :].rearrange("p (k f) -> p k f", k=KC),
                                  chunk(wu[:, 0], f).bitcast(F32), ALU.subtract)
                dve.tensor_tensor(wd[:, 1, f, :], piece[i][:, 2, :], wd[:, 0, f, :].bitcast(F32),
                                  ALU.subtract).then_inc(w_lo, 1)

            piece_lo(0)
            piece_lo(1)
            hidden(0, 0, 0)

            def one_round(b, half, more, r):
                for f in range(NFS):
                    hidden_lo(b, half, f)
                    j = f // 2
                    if j < NT:
                        if f % 2 == 0:
                            attention_stats(b, j)
                            if j:
                                for k in range(TOPK):
                                    add_expert(b, j - 1, k)
                        else:
                            add_attention(b, j)
                    if f == 2 * NT:
                        for k in range(TOPK):
                            add_expert(b, NT - 1, k)
                    if f + 1 < NFS:
                        hidden(b, half, f + 1)
                    elif more:
                        hidden(b + 1, 1 - half, 0)
                    if isinstance(b, int) and b == 0 and f + 2 < NFS:
                        piece_lo(f + 2)
                for j in range(NT):
                    finish(b, j)
                if more:
                    fetch_rec(b + 1)

            rounds(dve, one_round)

        @block.tensor
        def _(pe):
            def up_gate(b, half, f, r):
                n = b * NFS + f
                i = (half * NFS + f) % 2
                if f == 0:
                    pe.wait_ge(zT_loaded[half], (r + 1) * NT * 16)
                if isinstance(b, int) and b == 0:
                    pe.wait_ge(w_lo, f + 1)
                for w, bank, free, done in ((wg, gp, silu_made, gate_done), (wu, up, h_made, up_done)):
                    wait(pe, free, n - 1)
                    for q, (w_part, x_part) in enumerate(PRODUCTS):
                        for k in range(KC):
                            last = pe.matmul(bank[i][:], chunk(w[:, w_part], f)[:, k, :], zT[half][:, :, x_part, k, :],
                                             start=(q == 0 and k == 0), stop=(q == 2 and k == KC - 1))
                    last.then_inc(done, 1)

            def down(b, half, f):
                n = b * NFS + f
                i = (half * NFS + f) % 2
                pe.wait_ge(h_lo, n + 1)
                for j in range(NT):
                    if f == 0:
                        wait(pe, total_made, (b - 1) * NT + j + 1)
                    for q, (h_part, w_part) in enumerate(PRODUCTS):
                        last = pe.matmul(yp[j][:], h[:, i, h_part, j * P:(j + 1) * P], wd[:, w_part, f, :],
                                         start=(f == 0 and q == 0), stop=(f == NFS - 1 and q == 2))
                    if f == NFS - 1:
                        last.then_inc(y_done, 1)
                if f < NFS - 1:
                    last.then_inc(h_used, 1)

            up_gate(0, 0, 0, 0)

            def one_round(b, half, more, r):
                for f in range(NFS):
                    if f + 1 < NFS:
                        up_gate(b, half, f + 1, r)
                    elif more:
                        up_gate(b + 1, 1 - half, 0, r + half)
                    down(b, half, f)

            rounds(pe, one_round)


def rwkv_moe_kernel(nc, a, out):
    tokens = B * T
    z_rows = nc.dram_tensor("z_rows", [tokens, C], F32).ap()
    zT = nc.dram_tensor("zT_tiles", [B, NT, P, 2 * KC * P], F32).ap()
    o_rows = nc.dram_tensor("o_rows", [tokens, C], F32).ap()
    y_rows = nc.dram_tensor("y_rows", [SLOTS, C], F32).ap()
    slots = nc.dram_tensor("slot_tokens", [SLOTS, 1], U32).ap()

    x_t = a["x"].rearrange("b (j p) c -> b j p c", p=P)
    o_t = o_rows.rearrange("(b j p) c -> b j p c", b=B, p=P)
    z_t = z_rows.rearrange("(b j p) c -> b j p c", b=B, p=P)
    out_t = out.rearrange("b (j p) c -> b j p c", p=P)
    y_p = y_rows.rearrange("(p s) c -> p (s c)", p=P)
    wg = a["w_gate"].rearrange("e (p k) f -> e p (k f)", k=KC)
    wu = a["w_up"].rearrange("e (p k) f -> e p (k f)", k=KC)
    whole = (len(FT) - 1) * P
    wd_a = a["w_down"][:, 0:whole, :].rearrange("e (f p) c -> e p f c", p=P)
    wd_b = a["w_down"][:, whole:F, :]

    def one(view):
        return lambda b, j: view[bass.ds(b, 1), j].rearrange("o p c -> (o p) c")

    def of_expert(view, form):
        return lambda e: view[bass.ds(e, 1)].rearrange(form)

    d = dict(a)
    d.update(
        x_tile=one(x_t), o_tile=one(o_t), z_tile=one(z_t), out_tile=one(out_t), zT_tile=one(zT),
        z_rows=z_rows, y_flat=y_rows, slots=slots, table=slots.rearrange("(p s) o -> p (s o)", p=P),
        w_gate=of_expert(wg, "o p n -> (o p) n"), w_up=of_expert(wu, "o p n -> (o p) n"),
        w_down_a=of_expert(wd_a, "o p f c -> (o p) f c"), w_down_b=of_expert(wd_b, "o p c -> (o p) c"),
        y_rows=lambda e: y_p[:, bass.ds(e * (NCT * C), NCT * C)],
    )
    with ExitStack() as ctx:
        keep = {
            "rec": ctx.enter_context(nc.sbuf_tensor("keep_rec", [P, B * REC], F32)),
            "slot": ctx.enter_context(nc.sbuf_tensor("keep_slot", [P, B * NT * TOPK], U32)),
        }
        attention_stage(nc, keep, d)
        expert_stage(nc, keep, d)
        output_stage(nc, keep, d)


def constants():
    r = np.arange(P, dtype=np.float32)
    token = np.arange(NT, dtype=np.float32)[None, :] * P + r[:, None] - T
    return np.concatenate([np.eye(P, dtype=np.float32), (r[:, None] < r[None, :]).astype(np.float32),
                           np.broadcast_to(np.arange(E, dtype=np.float32), (P, E)), token], axis=1)


def kernel(**inputs):
    import concourse.bacc as bacc
    from concourse.bass_utils import run_bass_kernel_spmd

    nc = bacc.Bacc("TRN2", target_bir_lowering=False, num_devices=1)
    arrays, args = {}, {}

    def give(name, a):
        a = np.ascontiguousarray(a)
        arrays["in_" + name] = a
        args[name] = nc.dram_tensor("in_" + name, a.shape, mybir.dt.from_np(a.dtype), kind="ExternalInput").ap()

    for name in ("x", "time_decay", "time_first", "tm_k", "tm_v", "tm_r", "tm_g", "ln_g", "ln_b"):
        give(name, inputs["L0_attn_" + name])
    for name in ("Wr", "Wk", "Wv", "Wg", "Wo"):
        give(name, np.asarray(inputs["L0_attn_" + name]).T)
    for name in ("w_norm", "w_router", "w_gate", "w_up", "w_down", "sw_gate", "sw_up", "sw_down", "w_shared_gate"):
        give(name, inputs["L0_ffn_" + name])
    give("const", constants())
    out = nc.dram_tensor("out", [B, T, C], F32, kind="ExternalOutput").ap()
    rwkv_moe_kernel(nc, args, out)
    r = run_bass_kernel_spmd(nc, [arrays], core_ids=[0])
    return r.results[0]["out"]
```
